# Optimizing a Trainium2 kernel written in Bass

```python
import numpy as np
import jax
import jax.numpy as jnp

def _softmax(x, axis=-1):
    return jax.nn.softmax(x, axis=axis)

def _gelu(x):
    return jax.nn.gelu(x, approximate=True)

def _silu(x):
    return jax.nn.silu(x)

def _sigmoid(x):
    return jax.nn.sigmoid(x)

def _layernorm(x, axis=-1, eps=1e-05):
    m = jnp.mean(x, axis=axis, keepdims=True)
    v = jnp.var(x, axis=axis, keepdims=True)
    return (x - m) / jnp.sqrt(v + eps)

def _scatter_add(tgt, idx, src, axis=0):
    return tgt.at[idx].add(src)

def _segment_sum(src, seg, n):
    return jax.ops.segment_sum(src, seg, n)
kernel_name = 'mk_dlrm_tower_d1_rec_r8_53db66'

def setup_inputs(seed: int=0):
    np.random.seed(seed)
    _w = jnp.asarray

    def _rec_inputs():
        import jax
        import jax.numpy as jnp
        _tk = jax.random.key(seed)
        dense_ctx = jax.random.normal(jax.random.fold_in(_tk, 190), (512, 16), jnp.float32)
        ids = jnp.stack([jax.random.randint(jax.random.fold_in(_tk, 200 + f), (512,), 0, v, jnp.int32) for f, v in enumerate([1000, 125000, 1000, 125000, 125000, 1250, 1000, 1250, 1000, 1000, 1250, 1000, 12500, 1250, 12500, 1250, 1250, 12500, 1250, 12500, 1000, 1250, 12500, 12500, 1000, 1000, 1000, 1250, 1250, 1250, 1000, 12500])], axis=1)
        tbl_0 = 0.05 * jax.random.normal(jax.random.fold_in(_tk, 500 + 0), (1000, 64), jnp.float32)
        tbl_1 = 0.05 * jax.random.normal(jax.random.fold_in(_tk, 500 + 1), (125000, 64), jnp.float32)
        tbl_2 = 0.05 * jax.random.normal(jax.random.fold_in(_tk, 500 + 2), (1000, 64), jnp.float32)
        tbl_3 = 0.05 * jax.random.normal(jax.random.fold_in(_tk, 500 + 3), (125000, 64), jnp.float32)
        tbl_4 = 0.05 * jax.random.normal(jax.random.fold_in(_tk, 500 + 4), (125000, 64), jnp.float32)
        tbl_5 = 0.05 * jax.random.normal(jax.random.fold_in(_tk, 500 + 5), (1250, 64), jnp.float32)
        tbl_6 = 0.05 * jax.random.normal(jax.random.fold_in(_tk, 500 + 6), (1000, 64), jnp.float32)
        tbl_7 = 0.05 * jax.random.normal(jax.random.fold_in(_tk, 500 + 7), (1250, 64), jnp.float32)
        tbl_8 = 0.05 * jax.random.normal(jax.random.fold_in(_tk, 500 + 8), (1000, 64), jnp.float32)
        tbl_9 = 0.05 * jax.random.normal(jax.random.fold_in(_tk, 500 + 9), (1000, 64), jnp.float32)
        tbl_10 = 0.05 * jax.random.normal(jax.random.fold_in(_tk, 500 + 10), (1250, 64), jnp.float32)
        tbl_11 = 0.05 * jax.random.normal(jax.random.fold_in(_tk, 500 + 11), (1000, 64), jnp.float32)
        tbl_12 = 0.05 * jax.random.normal(jax.random.fold_in(_tk, 500 + 12), (12500, 64), jnp.float32)
        tbl_13 = 0.05 * jax.random.normal(jax.random.fold_in(_tk, 500 + 13), (1250, 64), jnp.float32)
        tbl_14 = 0.05 * jax.random.normal(jax.random.fold_in(_tk, 500 + 14), (12500, 64), jnp.float32)
        tbl_15 = 0.05 * jax.random.normal(jax.random.fold_in(_tk, 500 + 15), (1250, 64), jnp.float32)
        tbl_16 = 0.05 * jax.random.normal(jax.random.fold_in(_tk, 500 + 16), (1250, 64), jnp.float32)
        tbl_17 = 0.05 * jax.random.normal(jax.random.fold_in(_tk, 500 + 17), (12500, 64), jnp.float32)
        tbl_18 = 0.05 * jax.random.normal(jax.random.fold_in(_tk, 500 + 18), (1250, 64), jnp.float32)
        tbl_19 = 0.05 * jax.random.normal(jax.random.fold_in(_tk, 500 + 19), (12500, 64), jnp.float32)
        tbl_20 = 0.05 * jax.random.normal(jax.random.fold_in(_tk, 500 + 20), (1000, 64), jnp.float32)
        tbl_21 = 0.05 * jax.random.normal(jax.random.fold_in(_tk, 500 + 21), (1250, 64), jnp.float32)
        tbl_22 = 0.05 * jax.random.normal(jax.random.fold_in(_tk, 500 + 22), (12500, 64), jnp.float32)
        tbl_23 = 0.05 * jax.random.normal(jax.random.fold_in(_tk, 500 + 23), (12500, 64), jnp.float32)
        tbl_24 = 0.05 * jax.random.normal(jax.random.fold_in(_tk, 500 + 24), (1000, 64), jnp.float32)
        tbl_25 = 0.05 * jax.random.normal(jax.random.fold_in(_tk, 500 + 25), (1000, 64), jnp.float32)
        tbl_26 = 0.05 * jax.random.normal(jax.random.fold_in(_tk, 500 + 26), (1000, 64), jnp.float32)
        tbl_27 = 0.05 * jax.random.normal(jax.random.fold_in(_tk, 500 + 27), (1250, 64), jnp.float32)
        tbl_28 = 0.05 * jax.random.normal(jax.random.fold_in(_tk, 500 + 28), (1250, 64), jnp.float32)
        tbl_29 = 0.05 * jax.random.normal(jax.random.fold_in(_tk, 500 + 29), (1250, 64), jnp.float32)
        tbl_30 = 0.05 * jax.random.normal(jax.random.fold_in(_tk, 500 + 30), (1000, 64), jnp.float32)
        tbl_31 = 0.05 * jax.random.normal(jax.random.fold_in(_tk, 500 + 31), (12500, 64), jnp.float32)
        _rk = jax.random.fold_in(_tk, 7)
        W_top1 = 0.0441942 * jax.random.normal(jax.random.fold_in(_tk, 801), (512, 512), jnp.float32)
        W_top2 = 0.0441942 * jax.random.normal(jax.random.fold_in(_tk, 802), (512, 256), jnp.float32)
        W_top3 = 0.0625 * jax.random.normal(jax.random.fold_in(_tk, 803), (256, 1), jnp.float32)
        b_top1 = jnp.zeros((512,), jnp.float32)
        b_top2 = jnp.zeros((256,), jnp.float32)
        return (dense_ctx, ids, tbl_0, tbl_1, tbl_2, tbl_3, tbl_4, tbl_5, tbl_6, tbl_7, tbl_8, tbl_9, tbl_10, tbl_11, tbl_12, tbl_13, tbl_14, tbl_15, tbl_16, tbl_17, tbl_18, tbl_19, tbl_20, tbl_21, tbl_22, tbl_23, tbl_24, tbl_25, tbl_26, tbl_27, tbl_28, tbl_29, tbl_30, tbl_31, W_top1, b_top1, W_top2, b_top2, W_top3)
    dense_ctx, ids, tbl_0, tbl_1, tbl_2, tbl_3, tbl_4, tbl_5, tbl_6, tbl_7, tbl_8, tbl_9, tbl_10, tbl_11, tbl_12, tbl_13, tbl_14, tbl_15, tbl_16, tbl_17, tbl_18, tbl_19, tbl_20, tbl_21, tbl_22, tbl_23, tbl_24, tbl_25, tbl_26, tbl_27, tbl_28, tbl_29, tbl_30, tbl_31, W_top1, b_top1, W_top2, b_top2, W_top3 = _rec_inputs()

    def _L0_rec_setup():
        import jax, jax.numpy as jnp
        import numpy as np
        BATCH = 1024
        NUM_FIELDS = 32
        EMBED_DIM = 64
        NUM_IX = NUM_FIELDS * (NUM_FIELDS - 1) // 2
        key = jax.random.key(seed)
        kx, kk = jax.random.split(key)
        x = jax.random.normal(kx, (BATCH, NUM_FIELDS, EMBED_DIM), dtype=jnp.float32)
        fan = EMBED_DIM + EMBED_DIM
        limit = float(np.sqrt(6.0 / fan))
        kernel = jax.random.uniform(kk, (EMBED_DIM, NUM_IX, EMBED_DIM), dtype=jnp.float32, minval=-limit, maxval=limit)
        return {'x': x, 'kernel': kernel}
    _L0_rec_all = _L0_rec_setup()
    _L0_rec_in = {k: v for k, v in _L0_rec_all.items() if k in ('kernel',)}
    del _L0_rec_all
    return {'dense_ctx': dense_ctx, 'ids': ids, 'tbl_0': tbl_0, 'tbl_1': tbl_1, 'tbl_2': tbl_2, 'tbl_3': tbl_3, 'tbl_4': tbl_4, 'tbl_5': tbl_5, 'tbl_6': tbl_6, 'tbl_7': tbl_7, 'tbl_8': tbl_8, 'tbl_9': tbl_9, 'tbl_10': tbl_10, 'tbl_11': tbl_11, 'tbl_12': tbl_12, 'tbl_13': tbl_13, 'tbl_14': tbl_14, 'tbl_15': tbl_15, 'tbl_16': tbl_16, 'tbl_17': tbl_17, 'tbl_18': tbl_18, 'tbl_19': tbl_19, 'tbl_20': tbl_20, 'tbl_21': tbl_21, 'tbl_22': tbl_22, 'tbl_23': tbl_23, 'tbl_24': tbl_24, 'tbl_25': tbl_25, 'tbl_26': tbl_26, 'tbl_27': tbl_27, 'tbl_28': tbl_28, 'tbl_29': tbl_29, 'tbl_30': tbl_30, 'tbl_31': tbl_31, 'W_top1': W_top1, 'b_top1': b_top1, 'W_top2': W_top2, 'b_top2': b_top2, 'W_top3': W_top3, 'L0_rec_kernel': _L0_rec_in['kernel']}

def reference(dense_ctx, ids, tbl_0, tbl_1, tbl_2, tbl_3, tbl_4, tbl_5, tbl_6, tbl_7, tbl_8, tbl_9, tbl_10, tbl_11, tbl_12, tbl_13, tbl_14, tbl_15, tbl_16, tbl_17, tbl_18, tbl_19, tbl_20, tbl_21, tbl_22, tbl_23, tbl_24, tbl_25, tbl_26, tbl_27, tbl_28, tbl_29, tbl_30, tbl_31, W_top1, b_top1, W_top2, b_top2, W_top3, L0_rec_kernel):
    import jax
    import jax.numpy as jnp

    def _L0_rec_ref(x, kernel):
        import jax, jax.numpy as jnp
        import numpy as np
        BATCH = 1024
        NUM_FIELDS = 32
        EMBED_DIM = 64
        NUM_IX = NUM_FIELDS * (NUM_FIELDS - 1) // 2
        num_fields = x.shape[1]
        row, col = np.triu_indices(num_fields, k=1)
        p = x[:, row]
        q = x[:, col]
        out = jnp.einsum('bni,oni,bno->bn', p, kernel, q)
        return out
    e = jnp.stack([tbl_0[ids[:, 0]], tbl_1[ids[:, 1]], tbl_2[ids[:, 2]], tbl_3[ids[:, 3]], tbl_4[ids[:, 4]], tbl_5[ids[:, 5]], tbl_6[ids[:, 6]], tbl_7[ids[:, 7]], tbl_8[ids[:, 8]], tbl_9[ids[:, 9]], tbl_10[ids[:, 10]], tbl_11[ids[:, 11]], tbl_12[ids[:, 12]], tbl_13[ids[:, 13]], tbl_14[ids[:, 14]], tbl_15[ids[:, 15]], tbl_16[ids[:, 16]], tbl_17[ids[:, 17]], tbl_18[ids[:, 18]], tbl_19[ids[:, 19]], tbl_20[ids[:, 20]], tbl_21[ids[:, 21]], tbl_22[ids[:, 22]], tbl_23[ids[:, 23]], tbl_24[ids[:, 24]], tbl_25[ids[:, 25]], tbl_26[ids[:, 26]], tbl_27[ids[:, 27]], tbl_28[ids[:, 28]], tbl_29[ids[:, 29]], tbl_30[ids[:, 30]], tbl_31[ids[:, 31]]], axis=1)
    z = _L0_rec_ref(e, L0_rec_kernel)
    z = z.reshape(z.shape[0], -1)
    h = jnp.concatenate([z, dense_ctx], axis=1)
    h = jnp.maximum(h @ W_top1 + b_top1, 0.0)
    h = jnp.maximum(h @ W_top2 + b_top2, 0.0)
    y = h @ W_top3
    return y

_drawn_inputs = setup_inputs


def setup_inputs(seed=0):
    import zlib

    import numpy as np

    out = dict(_drawn_inputs(seed))
    spreads = {'b_top1': (0.0, 0.1), 'b_top2': (0.0, 0.1)}
    factors = {'tbl_0': 2.78, 'tbl_17': 2.683}
    for name, (base, spread) in spreads.items():
        noise = np.random.default_rng([zlib.crc32(name.encode()), seed]).standard_normal(out[name].shape)
        drawn = base * np.exp(spread * noise) if base else spread * noise
        out[name] = jnp.asarray(drawn.astype(out[name].dtype))
    for name, factor in factors.items():
        out[name] = (out[name] * factor).astype(out[name].dtype)
    return out
```

```python
import numpy as np

import concourse.bass as bass
from concourse import mybir
from contextlib import ExitStack

B, F, D = 512, 32, 64
P = 128
BT = B // P
NK = F // 2
DENSE, H1, H2 = 16, 512, 256
TILES = [(k, j) for k in range(NK) for j in range(k + 1)]
FIRST = [k * (k + 1) // 2 for k in range(NK + 1)]
NT = len(TILES)
TG = 4
NG = NT // TG
GW = TG * P
W_SLOTS = 4
RAW_SLOTS = 3
P_SLOTS = 4
X_SLOTS = 4
UNITS_PER_BANK = 64
LAST_BANK = 3


def z_units():
    out, u = [], 0
    for k, j in TILES:
        if j == k:
            out.append([(1, LAST_BANK, k % 4, 24 + k // 4)])
            continue
        units = []
        for side in range(2):
            w = u % UNITS_PER_BANK
            units.append((side, u // UNITS_PER_BANK, w % 4, 2 * (w // 4)))
            u += 1
        out.append(units)
    return out


Z_UNITS = z_units()
LAST_TILE = {(q, grp): m for m in range(NT) for _, q, grp, _ in Z_UNITS[m]}
BANK_FULL = [max(LAST_TILE[q, grp] for grp in range(4)) + 1 for q in range(LAST_BANK + 1)]


def lead(k):
    return 0 if k < 6 else 3


def plan():
    weights = [[] for _ in range(NT + 1)]
    fields = [[] for _ in range(NT + 1)]
    banks = [[] for _ in range(NT + 1)]
    for g in range(NG):
        weights[max(0, TG * (g - W_SLOTS + 1) + 1)].append(g)
    for k in range(NK):
        fields[FIRST[k] - lead(k)] += [2 * k, 2 * k + 1]
    for q in range(LAST_BANK):
        banks[BANK_FULL[q] + 3].append(q)
    return weights, fields, banks


WEIGHTS_AT, FIELDS_AT, BANKS_AT = plan()


def tower(nc, ids, tables, kp, w1, b1, w2, b2, w3, dense_t, ident, ones, dense_sel, out):
    f32, f32r, i32 = mybir.dt.float32, mybir.dt.float32r, mybir.dt.int32
    ALU, ACT = mybir.AluOpType, mybir.ActivationFunctionType
    with ExitStack() as ctx:
        def sb(name, shape, dt=f32):
            return ctx.enter_context(nc.sbuf_tensor(name, shape, dt))

        def pb(name, shape):
            return ctx.enter_context(nc.psum_tensor(name, shape, f32))

        def sem(name):
            return ctx.enter_context(nc.semaphore(name))

        idx = sb("idx", [P, BT, F], i32)
        rows = sb("rows", [P, F, BT, 2, D])
        ident_sb = sb("ident_sb", [P, P])
        ones_sb = sb("ones_sb", [P, 62])
        dense_sel_sb = sb("dense_sel_sb", [DENSE, 4, 32])
        dense_sb = sb("dense_sb", [DENSE, B])
        x = sb("x", [P, X_SLOTS, 2, B], f32r)
        e_pair = sb("e_pair", [P, NK, B])
        raw = sb("raw", [P, RAW_SLOTS, 2, GW])
        k_high = sb("k_high", [P, 2, GW], f32r)
        k_low = sb("k_low", [P, 2, GW], f32r)
        w_a = sb("w_a", [P, W_SLOTS, GW], f32r)
        w_b = sb("w_b", [P, W_SLOTS, GW], f32r)
        prod = sb("prod", [P, P_SLOTS, 2, B])
        z = sb("z", [P, 4, B])
        w1_sb = sb("w1_sb", [P, 4, H1])
        w2_sb = sb("w2_sb", [P, H1 // P, H2])
        w3_sb = sb("w3_sb", [P, H2 // P])
        b1_sb = sb("b1_sb", [P, H1 // P])
        b2_sb = sb("b2_sb", [P, H2 // P])
        h1 = sb("h1", [P, H1 // P, B])
        h2 = sb("h2", [P, H2 // P, B])
        y = sb("y", [1, B])

        u_ps = pb("u_ps", [P, 2, 2, B])
        t_ps = pb("t_ps", [P, 2, B])
        z_ps = pb("z_ps", [P, B])
        z_last_ps = pb("z_last_ps", [P, B])
        h1_ps = u_ps[:].rearrange("p a b n -> p (a b) n")

        ids_in = sem("ids_in")
        consts_in = sem("consts_in")
        mlp_in = sem("mlp_in")
        gathered = [sem(f"gathered_{c}") for c in range(F)]
        raw_in = [sem(f"raw_in_{s}") for s in range(RAW_SLOTS)]
        low_placed = [sem(f"low_placed_{s}") for s in range(W_SLOTS)]
        k_high_done = sem("k_high_done")
        k_low_done = sem("k_low_done")
        high_placed = sem("high_placed")
        doubled = sem("doubled")
        transposed = sem("transposed")
        e_done = sem("e_done")
        x_done = sem("x_done")
        u_done = sem("u_done")
        prod_done = sem("prod_done")
        summed = sem("summed")
        bank_out = sem("bank_out")
        h1_acc = sem("h1_acc")
        h1_done = sem("h1_done")
        h2_acc = sem("h2_acc")
        h2_done = sem("h2_done")
        y_acc = sem("y_acc")
        y_done = sem("y_done")
        stored = sem("stored")
        block = ctx.enter_context(nc.Block())

        @block.sync
        def _(sp):
            sp.dma_start(idx[:], ids.rearrange("(t p) f -> p t f", p=P)).then_inc(ids_in, 16)

            def load_raw(n):
                if n >= RAW_SLOTS:
                    sp.wait_ge(k_low_done, 2 * (n - RAW_SLOTS) + 2)
                    sp.wait_ge(high_placed, 2 * (n - RAW_SLOTS) + 2)
                sp.dma_start(raw[:, n % RAW_SLOTS, :, :].rearrange("p a n -> p (a n)"),
                             kp[:, 2 * GW * n:2 * GW * (n + 1)]).then_inc(raw_in[n % RAW_SLOTS], 16)

            load_raw(0)
            sp.dma_start(ident_sb[:], ident).then_inc(consts_in, 16)
            sp.dma_start(ones_sb[:], ones).then_inc(consts_in, 16)
            sp.dma_start(dense_sel_sb[:], dense_sel).then_inc(consts_in, 16)
            sp.dma_start(dense_sb[:], dense_t).then_inc(consts_in, 16)
            for n in range(1, RAW_SLOTS):
                load_raw(n)
            for g in range(NG):
                slot = g % W_SLOTS
                if g >= W_SLOTS:
                    sp.wait_ge(u_done, TG * (g - W_SLOTS + 1))
                sp.wait_ge(k_low_done, g + 1)
                sp.dma_start(w_a[D:P, slot, :].bitcast(f32), k_low[0:D, g % 2, :].bitcast(f32)).then_inc(low_placed[slot], 16)
                sp.dma_start(w_b[0:D, slot, :].bitcast(f32), k_low[D:P, g % 2, :].bitcast(f32)).then_inc(low_placed[slot], 16)
                if g % 2 == 1 and g // 2 + RAW_SLOTS < NG // 2:
                    load_raw(g // 2 + RAW_SLOTS)
                if g == W_SLOTS:
                    sp.dma_start(w1_sb[:], w1.rearrange("(q p) n -> p q n", p=P)).then_inc(mlp_in, 16)
                    sp.dma_start(w2_sb[:], w2.rearrange("(q p) n -> p q n", p=P)).then_inc(mlp_in, 16)
                    sp.dma_start(w3_sb[:], w3).then_inc(mlp_in, 16)
                    sp.dma_start(b1_sb[:], b1).then_inc(mlp_in, 16)
                    sp.dma_start(b2_sb[:], b2).then_inc(mlp_in, 16)
            sp.wait_ge(y_done, 1)
            sp.dma_start(out, y[:]).then_inc(stored, 16)
            sp.wait_ge(stored, 16)

        @block.gpsimd
        def _(pool):
            pool.wait_ge(ids_in, 16)
            for c in range(F):
                for t in range(BT):
                    nc.gpsimd.indirect_dma_start(
                        out=rows[:, c, t, 0, :], out_offset=None, in_=tables[c],
                        in_offset=bass.IndirectOffsetOnAxis(ap=idx[:, t, c:c + 1], axis=0),
                    ).then_inc(gathered[c], 16)

        @block.scalar
        def _(act):
            def split_weights(g):
                load = g // 2
                act.wait_ge(raw_in[load % RAW_SLOTS], 16 * (load // RAW_SLOTS + 1))
                src = raw[:, load % RAW_SLOTS, g % 2, :]
                if g >= 2:
                    act.wait_ge(k_low_done, g - 1)
                nc.scalar.copy(k_high[:, g % 2, :], src).then_inc(k_high_done, 1)
                slot = g % W_SLOTS
                if g >= W_SLOTS:
                    act.wait_ge(u_done, TG * (g - W_SLOTS + 1))
                nc.scalar.copy(w_a[0:D, slot, :], src[0:D])
                nc.scalar.copy(w_b[D:P, slot, :], src[D:P]).then_inc(high_placed, 1)

            def double_field(c):
                act.wait_ge(gathered[c], 16 * BT)
                nc.scalar.copy(rows[:, c, :, 1, :], rows[:, c, :, 0, :]).then_inc(doubled, 1)

            def split_field(c):
                k = c // 2
                if k >= 2:
                    act.wait_ge(u_done, FIRST[k - 1])
                act.wait_ge(transposed, c + 1)
                nc.scalar.copy(x[:, c % X_SLOTS, 0, :], t_ps[:, c % 2, :])
                half = slice(0, D) if c % 2 == 0 else slice(D, P)
                nc.scalar.copy(e_pair[half, k, :], t_ps[half, c % 2, :]).then_inc(e_done, 1)

            for m in range(NT + 1):
                for g in WEIGHTS_AT[m]:
                    split_weights(g)
                for c in FIELDS_AT[m]:
                    double_field(c)
                for c in FIELDS_AT[m]:
                    split_field(c)
                for q in BANKS_AT[m]:
                    act.wait_ge(summed, BANK_FULL[q])
                    nc.scalar.copy(z[:, q, :], z_ps[:]).then_inc(bank_out, 1)
            act.wait_ge(summed, NT)
            nc.scalar.copy(z[:, LAST_BANK, :], z_last_ps[:]).then_inc(bank_out, 1)
            act.wait_ge(mlp_in, 5 * 16)
            for n in range(H1 // P):
                act.wait_ge(h1_acc, n + 1)
                nc.scalar.activation(h1[:, n, :], h1_ps[:, n, :], ACT.Relu,
                                     bias=b1_sb[:, n:n + 1]).then_inc(h1_done, 1)
            for n in range(H2 // P):
                act.wait_ge(h2_acc, n + 1)
                nc.scalar.activation(h2[:, n, :], t_ps[:, n, :], ACT.Relu,
                                     bias=b2_sb[:, n:n + 1]).then_inc(h2_done, 1)
            act.wait_ge(y_acc, 1)
            nc.scalar.copy(y[:], z_ps[0:1, :]).then_inc(y_done, 1)

        @block.vector
        def _(dve):
            def weights_low(g):
                load = g // 2
                dve.wait_ge(k_high_done, g + 1)
                if g >= 2:
                    dve.wait_ge(low_placed[(g - 2) % W_SLOTS], 32 * ((g - 2) // W_SLOTS + 1))
                nc.vector.tensor_tensor(k_low[:, g % 2, :], raw[:, load % RAW_SLOTS, g % 2, :],
                                        k_high[:, g % 2, :], ALU.subtract).then_inc(k_low_done, 1)

            def field_low(c):
                dve.wait_ge(e_done, c + 1)
                nc.vector.tensor_tensor(x[:, c % X_SLOTS, 1, :], t_ps[:, c % 2, :],
                                        x[:, c % X_SLOTS, 0, :], ALU.subtract).then_inc(x_done, 1)

            for m, (k, j) in enumerate(TILES):
                for g in WEIGHTS_AT[m]:
                    weights_low(g)
                for c in FIELDS_AT[m]:
                    field_low(c)
                dve.wait_ge(u_done, m + 1)
                if m >= P_SLOTS:
                    dve.wait_ge(summed, m - P_SLOTS + 1)
                if j == k:
                    dve.wait_ge(e_done, 2 * (k + 1))
                    nc.vector.tensor_tensor(prod[:, m % P_SLOTS, 1, :], u_ps[:, m % 2, 1, :],
                                            e_pair[:, j, :], ALU.mult).then_inc(prod_done, 1)
                else:
                    nc.vector.tensor_tensor(prod[:, m % P_SLOTS, :, :], u_ps[:, m % 2, :, :],
                                            e_pair[:, j:j + 1, :].broadcast_to([P, 2, B]),
                                            ALU.mult).then_inc(prod_done, 1)

        @block.tensor
        def _(pe):
            def transpose_field(c):
                pe.wait_ge(doubled, c + 1)
                if c >= 2:
                    pe.wait_ge(x_done, c - 1)
                    pe.wait_ge(e_done, c - 1)
                for t in range(BT):
                    last = nc.tensor.transpose(t_ps[:, c % 2, t * P:(t + 1) * P],
                                               rows[:, c, t, :, :].rearrange("p a d -> p (a d)"), ident_sb[:])
                last.then_inc(transposed, 1)

            def multiply(m):
                k, j = TILES[m]
                g, slot = m // TG, m // TG % W_SLOTS
                if j == 0:
                    pe.wait_ge(x_done, 2 * (k + 1))
                pe.wait_ge(high_placed, g + 1)
                pe.wait_ge(low_placed[slot], 32 * (g // W_SLOTS + 1))
                if m >= 2:
                    pe.wait_ge(prod_done, m - 1)
                cols = slice(m % TG * P, (m % TG + 1) * P)
                for side in ((1,) if j == k else (0, 1)):
                    w = (w_a, w_b)[side]
                    for part in range(2):
                        last = nc.tensor.matmul(u_ps[:, m % 2, side, :], w[:, slot, cols],
                                                x[:, (2 * k + side) % X_SLOTS, part, :],
                                                start=part == 0, stop=part == 1)
                last.then_inc(u_done, 1)

            def sum_tile(m):
                pe.wait_ge(prod_done, m + 1)
                for side, q, grp, row in Z_UNITS[m]:
                    if q == LAST_BANK:
                        dst, start, stop = z_last_ps, False, m == LAST_TILE[q, grp]
                    else:
                        dst, start, stop = z_ps, row == 0, m == LAST_TILE[q, grp]
                        if start and q > 0:
                            pe.wait_ge(bank_out, q)
                    last = nc.tensor.matmul(dst[32 * grp:32 * grp + 32, :], ones_sb[:, 30 - row:62 - row],
                                            prod[:, m % P_SLOTS, side, :], start=start, stop=stop)
                last.then_inc(summed, 1)

            def h1_part(q, n):
                return nc.tensor.matmul(h1_ps[:, n, :], w1_sb[:, q, n * P:(n + 1) * P], z[:, q, :],
                                        start=q == 0, stop=q == 3)

            pe.wait_ge(consts_in, 4 * 16)
            for grp in range(4):
                nc.tensor.matmul(z_last_ps[32 * grp:32 * grp + 32, :], dense_sel_sb[:, grp, :], dense_sb[:],
                                 start=True, stop=False)
            for m in range(NT):
                for c in FIELDS_AT[m]:
                    transpose_field(c)
                multiply(m)
                if m % 2 == 1 and m > 1:
                    sum_tile(m - 3)
                    sum_tile(m - 2)
            pe.wait_ge(mlp_in, 5 * 16)
            pe.wait_ge(bank_out, LAST_BANK)
            pe.wait_ge(prod_done, NT - 1)
            for n in range(2):
                for q in range(LAST_BANK):
                    h1_part(q, n)
            sum_tile(NT - 2)
            sum_tile(NT - 1)
            for n in range(2, H1 // P):
                for q in range(LAST_BANK):
                    h1_part(q, n)
            pe.wait_ge(bank_out, LAST_BANK + 1)
            for n in range(H1 // P):
                h1_part(LAST_BANK, n).then_inc(h1_acc, 1)
            for q in range(H1 // P):
                pe.wait_ge(h1_done, q + 1)
                for n in range(H2 // P):
                    last = nc.tensor.matmul(t_ps[:, n, :], w2_sb[:, q, n * P:(n + 1) * P], h1[:, q, :],
                                            start=q == 0, stop=q == H1 // P - 1)
                    if q == H1 // P - 1:
                        last.then_inc(h2_acc, 1)
            for n in range(H2 // P):
                pe.wait_ge(h2_done, n + 1)
                last = nc.tensor.matmul(z_ps[0:1, :], w3_sb[:, n:n + 1], h2[:, n, :],
                                        start=n == 0, stop=n == H2 // P - 1)
            last.then_inc(y_acc, 1)
    return nc


def pair_index(r, c):
    return r * F - r * (r + 1) // 2 + c - r - 1


def z_rows():
    at = -np.ones(4 * P, np.int64)
    for (k, j), units in zip(TILES, Z_UNITS):
        for side, q, grp, row in units:
            for r in range(2 * j, min(2 * j + 2, 2 * k + side)):
                at[q * P + 32 * grp + row + r - 2 * j] = pair_index(r, 2 * k + side)
    for d in range(DENSE):
        at[LAST_BANK * P + 32 * (d // 4) + 28 + d % 4] = F * (F - 1) // 2 + d
    return at


def pack_weights(k3):
    packed = np.zeros((2, D, NT, 2, D), k3.dtype)
    for m, (k, j) in enumerate(TILES):
        for side in range(2):
            for r in range(2 * j, min(2 * j + 2, 2 * k + side)):
                packed[side, :, m, r - 2 * j, :] = k3[:, pair_index(r, 2 * k + side), :]
    return packed.reshape(P, NT * P)


def kernel(**inputs):
    import concourse.bacc as bacc
    from concourse.bass_utils import run_bass_kernel_spmd

    given = {n: np.ascontiguousarray(a) for n, a in inputs.items()}
    w1 = given["W_top1"]
    at = z_rows()
    w1_rows = np.zeros((4 * P, H1), w1.dtype)
    w1_rows[at >= 0] = w1[at[at >= 0]]
    ones = np.zeros((P, 62), np.float32)
    ones[:D, 30] = 1
    ones[D:, 31] = 1
    dense_sel = np.zeros((DENSE, 4, 32), np.float32)
    for d in range(DENSE):
        dense_sel[d, d // 4, 28 + d % 4] = 1
    arrays = {"ids": given["ids"]}
    for c in range(F):
        arrays[f"tbl_{c}"] = given[f"tbl_{c}"]
    arrays |= {
        "kp": pack_weights(given["L0_rec_kernel"]),
        "w1": w1_rows,
        "b1": np.ascontiguousarray(given["b_top1"].reshape(H1 // P, P).T),
        "w2": given["W_top2"],
        "b2": np.ascontiguousarray(given["b_top2"].reshape(H2 // P, P).T),
        "w3": np.ascontiguousarray(given["W_top3"].reshape(H2 // P, P).T),
        "dense_t": np.ascontiguousarray(given["dense_ctx"].T),
        "ident": np.eye(P, dtype=np.float32),
        "ones": ones,
        "dense_sel": dense_sel,
    }
    nc = bacc.Bacc("TRN2", target_bir_lowering=False, num_devices=1)
    ap = {n: nc.dram_tensor(f"in_{n}", a.shape, mybir.dt.from_np(a.dtype), kind="ExternalInput").ap()
          for n, a in arrays.items()}
    out = nc.dram_tensor("out_y", (1, B), mybir.dt.float32, kind="ExternalOutput").ap()
    tables = [ap.pop(f"tbl_{c}") for c in range(F)]
    tower(nc, ap.pop("ids"), tables, **ap, out=out)
    result = run_bass_kernel_spmd(nc, [{f"in_{n}": a for n, a in arrays.items()}], core_ids=[0])
    return np.asarray(result.results[0]["out_y"]).reshape(B, 1)
```

```python
import numpy as np

import concourse.bass as bass
from concourse import mybir
from contextlib import ExitStack

B, F, D = 512, 32, 64
P = 128
BT = B // P
NK = F // 2
DENSE, H1, H2 = 16, 512, 256
TILES = [(k, j) for k in range(NK) for j in range(k + 1)]
FIRST = [k * (k + 1) // 2 for k in range(NK + 1)]
NT = len(TILES)
TG = 4
NG = NT // TG
GW = TG * P
W_SLOTS = 4
RAW_SLOTS = 3
P_SLOTS = 4
X_SLOTS = 3
ROW_SLOTS = 16
DVE_GROUPS = 18
U_SLOTS = 3
GROUPS, GROUP = 4, P // 4
BANKS = 4


def z_units():
    tiles, spare, bank, used, turn = [], [], 0, [0] * GROUPS, 0
    for k, j in TILES:
        sides = (1,) if j == k else (0, 1)
        size = 1 if j == k else 2
        for retry in range(2):
            units, now, at = [], list(used), turn
            for side in sides:
                open_groups = [(at + i) % GROUPS for i in range(GROUPS) if now[(at + i) % GROUPS] + size <= GROUP]
                if open_groups:
                    grp = open_groups[0]
                    units.append((side, bank, grp, now[grp]))
                    now[grp] += size
                    at = (grp + 1) % GROUPS
            if len(units) == len(sides):
                break
            spare += [(bank, grp, row) for grp in range(GROUPS) for row in range(used[grp], GROUP)]
            bank, used, turn = bank + 1, [0] * GROUPS, 0
        used, turn = now, at
        tiles.append(units)
    spare += [(bank, grp, row) for grp in range(GROUPS) for row in range(used[grp], GROUP)]
    assert bank == BANKS - 1 and len(spare) == DENSE
    return tiles, spare


Z_UNITS, DENSE_ROWS = z_units()
LAST_TILE = {(q, grp): m for m in range(NT) for _, q, grp, _ in Z_UNITS[m]}
BANK_FULL = [max(LAST_TILE[q, grp] for grp in range(GROUPS)) + 1 for q in range(BANKS)]
DENSE_GROUPS = sorted({(q, grp) for q, grp, _ in DENSE_ROWS})


def lead(k):
    return min(k, 4) if k < 7 else 7


def plan():
    weights = [[] for _ in range(NT + 1)]
    fields = [[] for _ in range(NT + 1)]
    banks = [[] for _ in range(NT + 1)]
    for g in range(NG):
        weights[max(0, TG * (g - W_SLOTS + 1) + 1)].append(g)
    for k in range(NK):
        fields[FIRST[k] - lead(k)].append(k)
    for q in range(BANKS - 1):
        banks[BANK_FULL[q] + 2].append(q)
    return weights, fields, banks


WEIGHTS_AT, FIELDS_AT, BANKS_AT = plan()


def pool_groups():
    after = [[] for _ in range(NK)]
    for g in range(min(DVE_GROUPS, NG), NG):
        after[NK - 1].append(g)
    return after


POOL_GROUPS_AFTER = pool_groups()


def tower(nc, ids, tables, kp, w1, b1, w2, b2, w3, dense_t, ident, ones, dense_sel, out):
    f32, f32r, i32 = mybir.dt.float32, mybir.dt.float32r, mybir.dt.int32
    ALU, ACT = mybir.AluOpType, mybir.ActivationFunctionType
    with ExitStack() as ctx:
        def sb(name, shape, dt=f32):
            return ctx.enter_context(nc.sbuf_tensor(name, shape, dt))

        def pb(name, shape):
            return ctx.enter_context(nc.psum_tensor(name, shape, f32))

        def sem(name):
            return ctx.enter_context(nc.semaphore(name))

        idx = sb("idx", [P, BT, F], i32)
        rows = sb("rows", [P, ROW_SLOTS, BT, 2, D])
        ident_sb = sb("ident_sb", [P, P])
        ones_sb = sb("ones_sb", [P, 2 * GROUP])
        dense_sel_sb = sb("dense_sel_sb", [DENSE, len(DENSE_GROUPS), GROUP])
        dense_sb = sb("dense_sb", [DENSE, B])
        e_split = sb("e_split", [P, 2, 2, B], f32r)
        x = sb("x", [P, X_SLOTS, 2, 2, B], f32r)
        e_pair = sb("e_pair", [P, NK, B])
        raw = sb("raw", [P, RAW_SLOTS, 2, GW])
        k_high = sb("k_high", [P, 2, GW], f32r)
        k_low = sb("k_low", [P, 2, GW], f32r)
        w_a = sb("w_a", [P, W_SLOTS, GW], f32r)
        w_b = sb("w_b", [P, W_SLOTS, GW], f32r)
        prod = sb("prod", [P, P_SLOTS, 2, B])
        z = sb("z", [P, 4, B])
        w1_sb = sb("w1_sb", [P, 4, H1])
        w2_sb = sb("w2_sb", [P, H1 // P, H2])
        w3_sb = sb("w3_sb", [P, H2 // P])
        b1_sb = sb("b1_sb", [P, H1 // P])
        b2_sb = sb("b2_sb", [P, H2 // P])
        h1 = sb("h1", [P, H1 // P, B])
        h2 = sb("h2", [P, H2 // P, B])
        y = sb("y", [1, B])

        u_ps = pb("u_ps", [P, U_SLOTS, 2, B])
        t_ps = pb("t_ps", [P, B])
        z_ps = pb("z_ps", [P, B])
        banks_ps = u_ps[:].rearrange("p a b n -> p (a b) n")
        h1_ps, h2_ps = banks_ps[:, 0:4, :], banks_ps[:, 4:6, :]

        ids_in = sem("ids_in")
        consts_in = sem("consts_in")
        mlp_in = sem("mlp_in")
        gathered = [sem(f"gathered_{k}") for k in range(NK)]
        raw_in = [sem(f"raw_in_{s}") for s in range(RAW_SLOTS)]
        low_placed = [sem(f"low_placed_{s}") for s in range(W_SLOTS)]
        k_high_done = sem("k_high_done")
        k_low_dve = sem("k_low_dve")
        k_low_pool = sem("k_low_pool")
        high_placed = sem("high_placed")
        transposed = sem("transposed")
        e_done = sem("e_done")
        e_low_done = sem("e_low_done")
        x_placed = [sem(f"x_placed_{s}") for s in range(X_SLOTS)]
        u_done = sem("u_done")
        prod_done = sem("prod_done")
        summed = sem("summed")
        bank_out = sem("bank_out")
        h1_acc = sem("h1_acc")
        h1_done = sem("h1_done")
        h2_acc = sem("h2_acc")
        h2_done = sem("h2_done")
        y_acc = sem("y_acc")
        y_done = sem("y_done")
        stored = sem("stored")
        block = ctx.enter_context(nc.Block())

        def k_low_done(g):
            return k_low_dve if g < DVE_GROUPS else k_low_pool

        def k_low_count(g):
            return g + 1 if g < DVE_GROUPS else g + 1 - DVE_GROUPS

        def weights_low(engine, arith, g):
            engine.wait_ge(k_high_done, g + 1)
            if g >= 2:
                engine.wait_ge(low_placed[(g - 2) % W_SLOTS], 32 * ((g - 2) // W_SLOTS + 1))
            arith.tensor_tensor(k_low[:, g % 2, :], raw[:, g // 2 % RAW_SLOTS, g % 2, :],
                                k_high[:, g % 2, :], ALU.subtract).then_inc(k_low_done(g), 1)

        @block.sync
        def _(sp):
            sp.dma_start(idx[:], ids.rearrange("(t p) f -> p t f", p=P)).then_inc(ids_in, 16)

            def load_raw(n):
                if n >= RAW_SLOTS:
                    last = 2 * (n - RAW_SLOTS) + 1
                    sp.wait_ge(k_low_done(last), k_low_count(last))
                    sp.wait_ge(high_placed, last + 1)
                sp.dma_start(raw[:, n % RAW_SLOTS, :, :].rearrange("p a n -> p (a n)"),
                             kp[:, 2 * GW * n:2 * GW * (n + 1)]).then_inc(raw_in[n % RAW_SLOTS], 16)

            load_raw(0)
            sp.dma_start(ident_sb[:], ident).then_inc(consts_in, 16)
            sp.dma_start(ones_sb[:], ones).then_inc(consts_in, 16)
            sp.dma_start(dense_sel_sb[:], dense_sel).then_inc(consts_in, 16)
            sp.dma_start(dense_sb[:], dense_t).then_inc(consts_in, 16)
            for n in range(1, RAW_SLOTS):
                load_raw(n)
            def place_weights(g):
                slot = g % W_SLOTS
                if g >= W_SLOTS:
                    sp.wait_ge(u_done, TG * (g - W_SLOTS + 1))
                sp.wait_ge(k_low_done(g), k_low_count(g))
                sp.dma_start(w_a[D:P, slot, :].bitcast(f32),
                             k_low[0:D, g % 2, :].bitcast(f32)).then_inc(low_placed[slot], 16)
                sp.dma_start(w_b[0:D, slot, :].bitcast(f32),
                             k_low[D:P, g % 2, :].bitcast(f32)).then_inc(low_placed[slot], 16)
                if g % 2 == 1 and g // 2 + RAW_SLOTS < NG // 2:
                    load_raw(g // 2 + RAW_SLOTS)

            def place_fields(k):
                slot = k % X_SLOTS
                if k >= X_SLOTS:
                    sp.wait_ge(u_done, FIRST[k - X_SLOTS + 1])
                sp.wait_ge(e_low_done, k + 1)
                for half in (slice(0, D), slice(D, P)):
                    for side, own in enumerate((slice(0, D), slice(D, P))):
                        sp.dma_start(x[half, slot, side, :, :].bitcast(f32),
                                     e_split[own, k % 2, :, :].bitcast(f32)).then_inc(x_placed[slot], 16)

            for m in range(NT):
                for g in WEIGHTS_AT[m]:
                    place_weights(g)
                for k in FIELDS_AT[m]:
                    place_fields(k)
                if m == 8:
                    sp.dma_start(w1_sb[:], w1.rearrange("(q p) n -> p q n", p=P)).then_inc(mlp_in, 16)
                    sp.dma_start(w2_sb[:], w2.rearrange("(q p) n -> p q n", p=P)).then_inc(mlp_in, 16)
                    sp.dma_start(w3_sb[:], w3).then_inc(mlp_in, 16)
                    sp.dma_start(b1_sb[:], b1).then_inc(mlp_in, 16)
                    sp.dma_start(b2_sb[:], b2).then_inc(mlp_in, 16)
            sp.wait_ge(y_done, 1)
            sp.dma_start(out, y[:]).then_inc(stored, 16)
            sp.wait_ge(stored, 16)

        @block.gpsimd
        def _(pool):
            pool.wait_ge(ids_in, 16)
            for k in range(NK):
                if k >= ROW_SLOTS:
                    pool.wait_ge(transposed, k - ROW_SLOTS + 1)
                for c in (2 * k, 2 * k + 1):
                    for t in range(BT):
                        nc.gpsimd.indirect_dma_start(
                            out=rows[:, k % ROW_SLOTS, t, c % 2, :], out_offset=None, in_=tables[c],
                            in_offset=bass.IndirectOffsetOnAxis(ap=idx[:, t, c:c + 1], axis=0),
                        ).then_inc(gathered[k], 16)
                for g in POOL_GROUPS_AFTER[k]:
                    weights_low(pool, nc.gpsimd, g)

        @block.scalar
        def _(act):
            def split_weights(g):
                load = g // 2
                act.wait_ge(raw_in[load % RAW_SLOTS], 16 * (load // RAW_SLOTS + 1))
                src = raw[:, load % RAW_SLOTS, g % 2, :]
                if g >= 2:
                    act.wait_ge(k_low_done(g - 2), k_low_count(g - 2))
                nc.scalar.copy(k_high[:, g % 2, :], src).then_inc(k_high_done, 1)
                slot = g % W_SLOTS
                if g >= W_SLOTS:
                    act.wait_ge(u_done, TG * (g - W_SLOTS + 1))
                nc.scalar.copy(w_a[0:D, slot, :], src[0:D])
                nc.scalar.copy(w_b[D:P, slot, :], src[D:P]).then_inc(high_placed, 1)

            def split_fields(k):
                if k >= 2:
                    act.wait_ge(x_placed[(k - 2) % X_SLOTS], 64 * ((k - 2) // X_SLOTS + 1))
                act.wait_ge(transposed, k + 1)
                nc.scalar.copy(e_split[:, k % 2, 0, :], t_ps[:])
                nc.scalar.copy(e_pair[:, k, :], t_ps[:]).then_inc(e_done, 1)

            for m in range(NT + 1):
                for g in WEIGHTS_AT[m]:
                    split_weights(g)
                for k in FIELDS_AT[m]:
                    split_fields(k)
                for q in BANKS_AT[m]:
                    act.wait_ge(summed, BANK_FULL[q])
                    nc.scalar.copy(z[:, q, :], z_ps[:]).then_inc(bank_out, 1)
            act.wait_ge(summed, NT)
            nc.scalar.copy(z[:, BANKS - 1, :], z_ps[:]).then_inc(bank_out, 1)
            act.wait_ge(mlp_in, 5 * 16)
            for n in range(H1 // P):
                act.wait_ge(h1_acc, n + 1)
                nc.scalar.activation(h1[:, n, :], h1_ps[:, n, :], ACT.Relu,
                                     bias=b1_sb[:, n:n + 1]).then_inc(h1_done, 1)
            for n in range(H2 // P):
                act.wait_ge(h2_acc, n + 1)
                nc.scalar.activation(h2[:, n, :], h2_ps[:, n, :], ACT.Relu,
                                     bias=b2_sb[:, n:n + 1]).then_inc(h2_done, 1)
            act.wait_ge(y_acc, 1)
            nc.scalar.copy(y[:], t_ps[0:1, :]).then_inc(y_done, 1)

        @block.vector
        def _(dve):
            def fields_low(k):
                dve.wait_ge(e_done, k + 1)
                nc.vector.tensor_tensor(e_split[:, k % 2, 1, :], e_pair[:, k, :], e_split[:, k % 2, 0, :],
                                        ALU.subtract).then_inc(e_low_done, 1)

            for m, (k, j) in enumerate(TILES):
                for g in WEIGHTS_AT[m]:
                    if g < DVE_GROUPS:
                        weights_low(dve, nc.vector, g)
                for b in FIELDS_AT[m]:
                    fields_low(b)
                dve.wait_ge(u_done, m + 1)
                if m >= P_SLOTS:
                    dve.wait_ge(summed, m - P_SLOTS + 1)
                if j == k:
                    dve.wait_ge(e_done, k + 1)
                    nc.vector.tensor_tensor(prod[:, m % P_SLOTS, 1, :], u_ps[:, m % U_SLOTS, 1, :],
                                            e_pair[:, j, :], ALU.mult).then_inc(prod_done, 1)
                else:
                    nc.vector.tensor_tensor(prod[:, m % P_SLOTS, :, :], u_ps[:, m % U_SLOTS, :, :],
                                            e_pair[:, j:j + 1, :].broadcast_to([P, 2, B]),
                                            ALU.mult).then_inc(prod_done, 1)

        @block.tensor
        def _(pe):
            def transpose_fields(k):
                pe.wait_ge(gathered[k], 2 * BT * 16)
                if k >= 1:
                    pe.wait_ge(e_done, k)
                for t in range(BT):
                    last = nc.tensor.transpose(t_ps[:, t * P:(t + 1) * P],
                                               rows[:, k % ROW_SLOTS, t, :, :].rearrange("p a d -> p (a d)"),
                                               ident_sb[:])
                last.then_inc(transposed, 1)

            def multiply(m):
                k, j = TILES[m]
                g, slot = m // TG, m // TG % W_SLOTS
                if j == 0:
                    pe.wait_ge(x_placed[k % X_SLOTS], 64 * (k // X_SLOTS + 1))
                pe.wait_ge(high_placed, g + 1)
                pe.wait_ge(low_placed[slot], 32 * (g // W_SLOTS + 1))
                if m >= U_SLOTS:
                    pe.wait_ge(prod_done, m - U_SLOTS + 1)
                cols = slice(m % TG * P, (m % TG + 1) * P)
                for side in ((1,) if j == k else (0, 1)):
                    w = (w_a, w_b)[side]
                    for part in range(2):
                        last = nc.tensor.matmul(u_ps[:, m % U_SLOTS, side, :], w[:, slot, cols],
                                                x[:, k % X_SLOTS, side, part, :],
                                                start=part == 0, stop=part == 1)
                last.then_inc(u_done, 1)

            def sum_tile(m):
                pe.wait_ge(prod_done, m + 1)
                if m in BANK_FULL:
                    pe.wait_ge(bank_out, Z_UNITS[m][0][1])
                if m == 0 or m in BANK_FULL:
                    bank = Z_UNITS[m][0][1]
                    for n, (q, grp) in enumerate(DENSE_GROUPS):
                        if q == bank:
                            nc.tensor.matmul(z_ps[GROUP * grp:GROUP * (grp + 1), :], dense_sel_sb[:, n, :],
                                             dense_sb[:], start=True, stop=False)
                for side, q, grp, row in Z_UNITS[m]:
                    last = nc.tensor.matmul(z_ps[GROUP * grp:GROUP * (grp + 1), :],
                                            ones_sb[:, GROUP - 1 - row:2 * GROUP - 1 - row],
                                            prod[:, m % P_SLOTS, side, :],
                                            start=row == 0 and (q, grp) not in DENSE_GROUPS,
                                            stop=m == LAST_TILE[q, grp])
                last.then_inc(summed, 1)

            def h1_part(q, n):
                return nc.tensor.matmul(h1_ps[:, n, :], w1_sb[:, q, n * P:(n + 1) * P], z[:, q, :],
                                        start=q == 0, stop=q == BANKS - 1)

            pe.wait_ge(consts_in, 4 * 16)
            for m in range(NT):
                for k in FIELDS_AT[m]:
                    transpose_fields(k)
                multiply(m)
                if m % 2 == 1 and m > 1:
                    sum_tile(m - 3)
                    sum_tile(m - 2)
            pe.wait_ge(mlp_in, 5 * 16)
            pe.wait_ge(bank_out, BANKS - 1)
            pe.wait_ge(prod_done, NT - 1)
            early = [n for n in range(H1 // P) if n // 2 != (NT - 1) % U_SLOTS]
            for n in early:
                for q in range(BANKS - 1):
                    h1_part(q, n)
            sum_tile(NT - 2)
            sum_tile(NT - 1)
            for n in range(H1 // P):
                if n not in early:
                    for q in range(BANKS - 1):
                        h1_part(q, n)
            pe.wait_ge(bank_out, BANKS)
            for n in range(H1 // P):
                h1_part(BANKS - 1, n).then_inc(h1_acc, 1)
            for q in range(H1 // P):
                pe.wait_ge(h1_done, q + 1)
                for n in range(H2 // P):
                    last = nc.tensor.matmul(h2_ps[:, n, :], w2_sb[:, q, n * P:(n + 1) * P], h1[:, q, :],
                                            start=q == 0, stop=q == H1 // P - 1)
                    if q == H1 // P - 1:
                        last.then_inc(h2_acc, 1)
            for n in range(H2 // P):
                pe.wait_ge(h2_done, n + 1)
                last = nc.tensor.matmul(t_ps[0:1, :], w3_sb[:, n:n + 1], h2[:, n, :],
                                        start=n == 0, stop=n == H2 // P - 1)
            last.then_inc(y_acc, 1)
    return nc


def pair_index(r, c):
    return r * F - r * (r + 1) // 2 + c - r - 1


def z_rows():
    at = np.full(BANKS * P, -1)
    for (k, j), units in zip(TILES, Z_UNITS):
        for side, q, grp, row in units:
            for r in range(2 * j, min(2 * j + 2, 2 * k + side)):
                at[q * P + GROUP * grp + row + r - 2 * j] = pair_index(r, 2 * k + side)
    for d, (q, grp, row) in enumerate(DENSE_ROWS):
        at[q * P + GROUP * grp + row] = F * (F - 1) // 2 + d
    return at


def pack_weights(k3):
    packed = np.zeros((2, D, NT, 2, D), k3.dtype)
    for m, (k, j) in enumerate(TILES):
        for side in range(2):
            for r in range(2 * j, min(2 * j + 2, 2 * k + side)):
                packed[side, :, m, r - 2 * j, :] = k3[:, pair_index(r, 2 * k + side), :]
    return packed.reshape(P, NT * P)


def kernel(**inputs):
    import concourse.bacc as bacc
    from concourse.bass_utils import run_bass_kernel_spmd

    given = {n: np.ascontiguousarray(a) for n, a in inputs.items()}
    ones = np.zeros((P, 2 * GROUP), np.float32)
    ones[:D, GROUP - 1] = 1
    ones[D:, GROUP] = 1
    dense_sel = np.zeros((DENSE, len(DENSE_GROUPS), GROUP), np.float32)
    for d, (q, grp, row) in enumerate(DENSE_ROWS):
        dense_sel[d, DENSE_GROUPS.index((q, grp)), row] = 1
    arrays = {"ids": given["ids"]}
    for c in range(F):
        arrays[f"tbl_{c}"] = given[f"tbl_{c}"]
    arrays |= {
        "kp": pack_weights(given["L0_rec_kernel"]),
        "w1": given["W_top1"][z_rows()],
        "b1": np.ascontiguousarray(given["b_top1"].reshape(H1 // P, P).T),
        "w2": given["W_top2"],
        "b2": np.ascontiguousarray(given["b_top2"].reshape(H2 // P, P).T),
        "w3": np.ascontiguousarray(given["W_top3"].reshape(H2 // P, P).T),
        "dense_t": np.ascontiguousarray(given["dense_ctx"].T),
        "ident": np.eye(P, dtype=np.float32),
        "ones": ones,
        "dense_sel": dense_sel,
    }
    nc = bacc.Bacc("TRN2", target_bir_lowering=False, num_devices=1)
    ap = {n: nc.dram_tensor(f"in_{n}", a.shape, mybir.dt.from_np(a.dtype), kind="ExternalInput").ap()
          for n, a in arrays.items()}
    out = nc.dram_tensor("out_y", (1, B), mybir.dt.float32, kind="ExternalOutput").ap()
    tables = [ap.pop(f"tbl_{c}") for c in range(F)]
    tower(nc, ap.pop("ids"), tables, **ap, out=out)
    result = run_bass_kernel_spmd(nc, [{f"in_{n}": a for n, a in arrays.items()}], core_ids=[0])
    return np.asarray(result.results[0]["out_y"]).reshape(B, 1)
```

```python
import numpy as np

import concourse.bass as bass
from concourse import mybir
from contextlib import ExitStack

B, F, D = 512, 32, 64
P = 128
BT = B // P
NK = F // 2
DENSE, H1, H2 = 16, 512, 256


def tile_units(k, j):
    if j == "single":
        return [(1, 2 * k - 1, (2 * k - 2, 2 * k + 1))]
    if j == "cross":
        return [(0, 2 * k, (2 * k - 2, 2 * k - 1)), (1, 2 * k + 1, (2 * k - 2, 2 * k))]
    return [(side, 2 * k + side, (2 * j, 2 * j + 1)) for side in range(2)]


TILES = [(k, j) for k in range(NK) for j in ["single", "cross"] * (k % 2) + list(range(k // 2 * 2))]
UNITS = [tile_units(k, j) for k, j in TILES]
FIRST = [sum(t[0] < k for t in TILES) for k in range(NK + 1)]
FIRST_UNIT = [sum(map(len, UNITS[:m])) for m in range(len(TILES) + 1)]
FIRST_USE = {c: m for m in reversed(range(len(TILES))) for _, c, _ in UNITS[m]}
LAST_USE = {c // 2: m for m in range(len(TILES)) for _, c, _ in UNITS[m]}
UNIT_AT = [(m, side) for m in range(len(TILES)) for side, _, _ in UNITS[m]]
NT = len(TILES)
TG = 4
NG = NT // TG
GW = TG * P
W_SLOTS = 4
RAW_SLOTS = 3
P_SLOTS = 4
X_SLOTS = 3
ROW_SLOTS = 11
HOT_BLOCKS = 3
HOT = 2 * HOT_BLOCKS
HOT_ROWS = 1000
HC = 8
HP = HOT_ROWS // HC
U_SLOTS = 3
GROUPS, GROUP = 4, P // 4
BANKS = 4
BANK_UNITS = P // 2
assert 2 * FIRST_UNIT[NT] + DENSE == BANKS * P
BANK_FULL = [next(m for m in range(NT + 1) if FIRST_UNIT[m] >= BANK_UNITS * (q + 1)) for q in range(BANKS - 1)]


def z_place(u):
    return u // BANK_UNITS, u % GROUPS, 2 * (u % BANK_UNITS // GROUPS)


DVE_PLACES = [(2, 1), (3, 1), (6, 0)]
POOL_LOWS = {0: HOT_BLOCKS, 1: HOT_BLOCKS} | {g: NK - 1 for g in range(24, NG)}
DVE_HIGHS = [2, 3]
LOW_AFTER = 1

STAGES = ("transpose", "split", "split_low", "mixed", "place_fields")
LEADS_EARLY = (8, 7, 5, 4, 4)
LEADS_LATE = (10, 9, 9, 6, 6)
EARLY_TASKS = [
    [("look_up", 0), ("look_up", 1), ("weights", 0), ("look_up", 2), ("look_up", 3), ("place_looked_up", 0),
     ("transpose", 3), ("looked_up_whole", 0), ("look_up", 4), ("place_looked_up", 1), ("looked_up_whole", 1),
     ("look_up", 5), ("weights", 1), ("weights", 2)],
    [("mixed", 0), ("split_low", 3), ("split", 3), ("place_looked_up", 2), ("looked_up_whole", 2),
     ("split_low", 4)],
    [("weights", 3), ("place_fields", 3), ("transpose", 4)],
    [],
    [("split", 4), ("place_fields", 4), ("mixed", 1)],
]


def plan():
    tasks = [[] for _ in range(NT + 1)]
    for m, early in enumerate(EARLY_TASKS):
        tasks[m] += early
    planned = sum(EARLY_TASKS, [])

    def add(m, task):
        if task not in planned:
            tasks[m].append(task)

    for g in range(W_SLOTS, NG):
        add(TG * (g - W_SLOTS + 1) + 1, ("weights", g))
    for k in range(HOT_BLOCKS, NK):
        for stage, tiles in zip(STAGES, LEADS_EARLY if k < 7 else LEADS_LATE):
            if stage != "mixed":
                add(FIRST[k] - tiles, (stage, k))
            elif k % 2 == 1:
                add(FIRST[k] - tiles, (stage, k // 2))
    for q in range(BANKS - 1):
        tasks[BANK_FULL[q] + 2].append(("bank", q))
    return tasks


TASKS = plan()


def tower(nc, order, ids, hot_ids, hot_base, tables, kp, w1, b1, w2, b2, w3, dense_t, ident, ones, dense_sel, out):
    f32, f32r, i32 = mybir.dt.float32, mybir.dt.float32r, mybir.dt.int32
    ALU, ACT = mybir.AluOpType, mybir.ActivationFunctionType
    with ExitStack() as ctx:
        def sb(name, shape, dt=f32):
            return ctx.enter_context(nc.sbuf_tensor(name, shape, dt))

        def pb(name, shape):
            return ctx.enter_context(nc.psum_tensor(name, shape, f32))

        def sem(name):
            return ctx.enter_context(nc.semaphore(name))

        idx = sb("idx", [P, BT, F], i32)
        rows = sb("rows", [P, ROW_SLOTS, BT, 2, D])
        ident_sb = sb("ident_sb", [P, P])
        ones_sb = sb("ones_sb", [P, 2 * GROUP])
        dense_sel_sb = sb("dense_sel_sb", [DENSE, GROUPS, GROUP])
        dense_sb = sb("dense_sb", [DENSE, B])
        e_split = sb("e_split", [P, 2, 2, B], f32r)
        x = sb("x", [P, X_SLOTS, 2, 2, B], f32r)
        e_pair = sb("e_pair", [P, NK, B])
        raw = sb("raw", [P, RAW_SLOTS, 2, GW])
        k_high = sb("k_high", [P, 2, GW], f32r)
        k_low = sb("k_low", [P, 2, GW], f32r)
        w_a = sb("w_a", [P, W_SLOTS, GW], f32r)
        w_b = sb("w_b", [P, W_SLOTS, GW], f32r)
        mixed = sb("mixed", [P, 2, B])
        prod = sb("prod", [P, P_SLOTS, 2, B])
        z = sb("z", [P, BANKS, B])
        w1_sb = sb("w1_sb", [P, 4, H1])
        w2_sb = sb("w2_sb", [P, H1 // P, H2])
        w3_sb = sb("w3_sb", [P, H2 // P])
        b1_sb = sb("b1_sb", [P, H1 // P])
        b2_sb = sb("b2_sb", [P, H2 // P])
        h1 = sb("h1", [P, H1 // P, B])
        h2 = sb("h2", [P, H2 // P, B])
        y = sb("y", [1, B])
        hot_w = sb("hot_w", [P, 2, HC, 2 * D], f32r)
        hot_one = sb("hot_one", [P, HC, B], f32r)
        hot_base_sb = sb("hot_base_sb", [P, 1])
        hot_raw = [h1[:, n, :] for n in range(4)] + [w1_sb[:, n, :] for n in range(2)]
        hot_id = [z[:, n, :].bitcast(i32) for n in range(4)] + [w1_sb[:, 2 + n, :].bitcast(i32) for n in range(2)]
        hot_diff = h2[:]

        u_ps = pb("u_ps", [P, U_SLOTS, 2, B])
        t_ps = pb("t_ps", [P, B])
        z_ps = pb("z_ps", [P, B])
        banks_ps = u_ps[:].rearrange("p a b n -> p (a b) n")
        h1_ps, h2_ps = banks_ps[:, 0:4, :], banks_ps[:, 4:6, :]

        ids_in = sem("ids_in")
        consts_in = sem("consts_in")
        mlp_in = sem("mlp_in")
        gathered = [sem(f"gathered_{k}") for k in range(NK)]
        raw_in = [sem(f"raw_in_{s}") for s in range(RAW_SLOTS)]
        low_placed = [sem(f"low_placed_{s}") for s in range(W_SLOTS)]
        k_high_done = sem("k_high_done")
        k_low_dve = sem("k_low_dve")
        k_low_pool = sem("k_low_pool")
        high_placed_act = sem("high_placed_act")
        high_placed_dve = sem("high_placed_dve")
        hot_ids_in = [sem(f"hot_ids_in_{n}") for n in range(HOT)]
        table_in = [sem(f"table_in_{n}") for n in range(HOT)]
        hot_base_in = sem("hot_base_in")
        y_zero = sem("y_zero")
        hot_diff_done = sem("hot_diff_done")
        hot_w_high = sem("hot_w_high")
        hot_w_done = sem("hot_w_done")
        hot_one_done = sem("hot_one_done")
        hot_used = sem("hot_used")
        transposed = sem("transposed")
        e_done = sem("e_done")
        looked_up_sum = sem("looked_up_sum")
        e_low_done = sem("e_low_done")
        mixed_done = sem("mixed_done")
        x_placed_act = sem("x_placed_act")
        x_placed_dve = sem("x_placed_dve")
        u_done = sem("u_done")
        prod_done = sem("prod_done")
        summed = sem("summed")
        bank_out = sem("bank_out")
        h1_acc = sem("h1_acc")
        h1_done = sem("h1_done")
        h2_acc = sem("h2_acc")
        h2_done = sem("h2_done")
        y_acc = sem("y_acc")
        y_done = sem("y_done")
        stored = sem("stored")
        block = ctx.enter_context(nc.Block())

        def looked_up_halves(k, side):
            return (slice(0, D),) if (k, side) == (0, 0) else (slice(0, D), slice(D, P))

        def looked_up_bank(n):
            return n // 2, n % 2

        def k_low_done(g):
            return k_low_pool if g in POOL_LOWS else k_low_dve

        def k_low_count(g):
            return sum((h in POOL_LOWS) == (g in POOL_LOWS) for h in range(g + 1))

        def weights_low(engine, arith, g):
            engine.wait_ge(k_high_done, g + 1)
            if g >= 2:
                engine.wait_ge(low_placed[(g - 2) % W_SLOTS], 32 * ((g - 2) // W_SLOTS + 1))
            arith.tensor_tensor(k_low[:, g % 2, :], raw[:, g // 2 % RAW_SLOTS, g % 2, :],
                                k_high[:, g % 2, :], ALU.subtract).then_inc(k_low_done(g), 1)

        def high_placed(g):
            if g in DVE_HIGHS:
                return high_placed_dve, sum(h in DVE_HIGHS for h in range(g + 1))
            return high_placed_act, sum(h not in DVE_HIGHS for h in range(g + 1))

        def x_placed(k, side):
            fields = [(i // 2, i % 2) for i in range(2 * k + side + 1)]
            if (k, side) in DVE_PLACES:
                return x_placed_dve, sum(f in DVE_PLACES for f in fields)
            return x_placed_act, sum(f not in DVE_PLACES for f in fields)

        @block.sync
        def _(sp):
            def load_table(n):
                sp.dma_start(hot_id[n], hot_ids[n:n + 1, :].broadcast_to([P, B])).then_inc(hot_ids_in[n], 16)
                sp.dma_start(hot_raw[n][0:HP, :],
                             tables[order[n]].rearrange("(p c) d -> p (c d)", c=HC)).then_inc(table_in[n], 16)

            def load_raw(n):
                if n >= RAW_SLOTS:
                    for g in (2 * (n - RAW_SLOTS), 2 * (n - RAW_SLOTS) + 1):
                        sp.wait_ge(k_low_done(g), k_low_count(g))
                        sp.wait_ge(*high_placed(g))
                sp.dma_start(raw[:, n % RAW_SLOTS, :, :].rearrange("p a n -> p (a n)"),
                             kp[:, 2 * GW * n:2 * GW * (n + 1)]).then_inc(raw_in[n % RAW_SLOTS], 16)

            load_table(0)
            sp.dma_start(idx[:], ids.rearrange("(t p) f -> p t f", p=P)).then_inc(ids_in, 16)
            load_table(1)
            load_raw(0)
            load_table(2)
            load_table(3)
            load_table(4)
            load_table(5)
            sp.dma_start(ident_sb[:], ident).then_inc(consts_in, 16)
            sp.dma_start(ones_sb[:], ones).then_inc(consts_in, 16)
            sp.dma_start(dense_sel_sb[:], dense_sel).then_inc(consts_in, 16)
            sp.dma_start(dense_sb[:], dense_t).then_inc(consts_in, 16)
            for n in range(1, RAW_SLOTS):
                load_raw(n)

            def place_weights(g):
                slot = g % W_SLOTS
                if g >= W_SLOTS:
                    sp.wait_ge(u_done, TG * (g - W_SLOTS + 1))
                sp.wait_ge(k_low_done(g), k_low_count(g))
                sp.dma_start(w_a[D:P, slot, :].bitcast(f32),
                             k_low[0:D, g % 2, :].bitcast(f32)).then_inc(low_placed[slot], 16)
                sp.dma_start(w_b[0:D, slot, :].bitcast(f32),
                             k_low[D:P, g % 2, :].bitcast(f32)).then_inc(low_placed[slot], 16)
                if g % 2 == 1 and g // 2 + RAW_SLOTS < NG // 2:
                    load_raw(g // 2 + RAW_SLOTS)

            for m in range(NT):
                for task, n in TASKS[m]:
                    if task == "weights":
                        place_weights(n)
                if m == 8:
                    sp.wait_ge(hot_diff_done, HOT)
                    sp.wait_ge(hot_w_done, HOT)
                    sp.dma_start(w1_sb[:], w1.rearrange("(q p) n -> p q n", p=P)).then_inc(mlp_in, 16)
                    sp.dma_start(w2_sb[:], w2.rearrange("(q p) n -> p q n", p=P)).then_inc(mlp_in, 16)
                    sp.dma_start(w3_sb[:], w3).then_inc(mlp_in, 16)
                    sp.dma_start(b1_sb[:], b1).then_inc(mlp_in, 16)
                    sp.dma_start(b2_sb[:], b2).then_inc(mlp_in, 16)
            sp.wait_ge(y_done, 1)
            sp.dma_start(out, y[:]).then_inc(stored, 16)
            sp.wait_ge(stored, 16)

        @block.gpsimd
        def _(pool):
            pool.wait_ge(ids_in, 16)
            for k in range(HOT_BLOCKS, NK):
                if k >= HOT_BLOCKS + ROW_SLOTS:
                    pool.wait_ge(transposed, k - HOT_BLOCKS - ROW_SLOTS + 1)
                for c in (2 * k, 2 * k + 1):
                    for t in range(BT):
                        nc.gpsimd.indirect_dma_start(
                            out=rows[:, k % ROW_SLOTS, t, c % 2, :], out_offset=None, in_=tables[order[c]],
                            in_offset=bass.IndirectOffsetOnAxis(ap=idx[:, t, order[c]:order[c] + 1], axis=0),
                        ).then_inc(gathered[k], 16)
                for g, after in POOL_LOWS.items():
                    if after == k:
                        weights_low(pool, nc.gpsimd, g)

        @block.scalar
        def _(act):
            act.dma_start(hot_base_sb[:], hot_base).then_inc(hot_base_in, 16)
            act.wait_ge(y_zero, 1)
            nc.scalar.activation(y[:, 0:1], y[:, 0:1], ACT.Identity)

            def look_up(n):
                if n == 0:
                    act.wait_ge(hot_base_in, 16)
                act.wait_ge(hot_ids_in[n], 16)
                if n >= 2:
                    act.wait_ge(hot_one_done, HC * (n - 1))
                nc.scalar.activation(hot_diff[0:HP, n % 2, :], hot_id[n][0:HP, :], ACT.Identity,
                                     bias=hot_base_sb[0:HP, :]).then_inc(hot_diff_done, 1)
                act.wait_ge(table_in[n], 16)
                if n >= 2:
                    act.wait_ge(hot_used, HC * (n - 1))
                nc.scalar.copy(hot_w[0:HP, n % 2, :, 0:D],
                               hot_raw[n][0:HP, :].rearrange("p (c d) -> p c d", c=HC)).then_inc(hot_w_high, 1)

            def place_looked_up(k):
                for side in range(2):
                    if (k, side) in DVE_PLACES:
                        continue
                    act.wait_ge(hot_used, HC * (2 * k + side + 1))
                    for part, have in enumerate((slice(0, D), slice(D, P))):
                        for half in looked_up_halves(k, side):
                            last = nc.scalar.copy(x[half, k % X_SLOTS, side, part, :],
                                                  u_ps[have, *looked_up_bank(2 * k + side), :])
                    last.then_inc(x_placed_act, 1)

            def weights_high(g):
                act.wait_ge(raw_in[g // 2 % RAW_SLOTS], 16 * (g // 2 // RAW_SLOTS + 1))
                if g >= 2:
                    act.wait_ge(k_low_done(g - 2), k_low_count(g - 2))
                nc.scalar.copy(k_high[:, g % 2, :],
                               raw[:, g // 2 % RAW_SLOTS, g % 2, :]).then_inc(k_high_done, 1)

            def place_weights(g):
                slot = g % W_SLOTS
                if g >= W_SLOTS:
                    act.wait_ge(u_done, TG * (g - W_SLOTS + 1))
                for w, own in ((w_a, slice(0, D)), (w_b, slice(D, P))):
                    last = nc.scalar.copy(w[own, slot, :], raw[own, g // 2 % RAW_SLOTS, g % 2, :])
                last.then_inc(high_placed_act, 1)

            def split_fields(k):
                act.wait_ge(transposed, k + 1 - HOT_BLOCKS)
                for side in range(2):
                    if k - 2 >= HOT_BLOCKS and (k - 2, side) in DVE_PLACES:
                        act.wait_ge(*x_placed(k - 2, side))
                nc.scalar.copy(e_split[:, k % 2, 0, :], t_ps[:])
                nc.scalar.copy(e_pair[:, k, :], t_ps[:]).then_inc(e_done, 1)

            def place_fields(k):
                if k >= X_SLOTS:
                    act.wait_ge(u_done, LAST_USE[k - X_SLOTS] + 1)
                act.wait_ge(e_low_done, k + 1 - HOT_BLOCKS)
                for side, own in enumerate((slice(0, D), slice(D, P))):
                    if (k, side) in DVE_PLACES:
                        continue
                    for half in (slice(0, D), slice(D, P)):
                        last = nc.scalar.copy(x[half, k % X_SLOTS, side, :, :], e_split[own, k % 2, :, :])
                    last.then_inc(x_placed_act, 1)

            def mix(p):
                k = 2 * p + 1
                act.wait_ge(looked_up_sum, min(k + 1, HOT_BLOCKS))
                if k >= HOT_BLOCKS:
                    act.wait_ge(e_done, k + 1 - HOT_BLOCKS)
                if p > 0:
                    act.wait_ge(prod_done, FIRST[k - 2] + 2)
                nc.scalar.copy(mixed[0:D, :, :], e_pair[0:D, k - 1:k, :].broadcast_to([D, 2, B]))
                nc.scalar.copy(mixed[D:P, 0, :], e_pair[0:D, k, :])
                nc.scalar.copy(mixed[D:P, 1, :], e_pair[D:P, k, :]).then_inc(mixed_done, 1)

            for m in range(NT + 1):
                for task, n in TASKS[m]:
                    if task == "mixed":
                        mix(n)
                    elif task == "weights":
                        if n == 0:
                            weights_high(0)
                        if n not in DVE_HIGHS:
                            place_weights(n)
                        if n + 1 < NG:
                            weights_high(n + 1)
                    elif task == "look_up":
                        look_up(n)
                    elif task == "place_looked_up":
                        place_looked_up(n)
                    elif task == "split":
                        split_fields(n)
                    elif task == "place_fields":
                        place_fields(n)
                    elif task == "bank":
                        act.wait_ge(summed, BANK_UNITS * (n + 1))
                        nc.scalar.copy(z[:, n, :], z_ps[:]).then_inc(bank_out, 1)
            act.wait_ge(summed, FIRST_UNIT[NT])
            nc.scalar.copy(z[:, BANKS - 1, :], z_ps[:]).then_inc(bank_out, 1)
            act.wait_ge(mlp_in, 5 * 16)
            for n in range(H1 // P):
                act.wait_ge(h1_acc, n + 1)
                nc.scalar.activation(h1[:, n, :], h1_ps[:, n, :], ACT.Relu,
                                     bias=b1_sb[:, n:n + 1]).then_inc(h1_done, 1)
            for n in range(H2 // P):
                act.wait_ge(h2_acc, n + 1)
                nc.scalar.activation(h2[:, n, :], h2_ps[:, n, :], ACT.Relu,
                                     bias=b2_sb[:, n:n + 1]).then_inc(h2_done, 1)
            act.wait_ge(y_acc, 1)
            nc.scalar.copy(y[:], t_ps[0:1, :]).then_inc(y_done, 1)

        @block.vector
        def _(dve):
            nc.vector.memset(y[:, 0:1], 0.0).then_inc(y_zero, 1)

            def look_up(n):
                dve.wait_ge(hot_diff_done, n + 1)
                for c in range(HC):
                    if n >= 1:
                        dve.wait_ge(hot_used, HC * (n - 1) + c + 1)
                    nc.vector.tensor_scalar(hot_one[0:HP, c, :], hot_diff[0:HP, n % 2, :], float(c), None,
                                            ALU.is_equal).then_inc(hot_one_done, 1)
                    if c == LOW_AFTER:
                        dve.wait_ge(hot_w_high, n + 1)
                        nc.vector.tensor_tensor(hot_w[0:HP, n % 2, :, D:2 * D],
                                                hot_raw[n][0:HP, :].rearrange("p (c d) -> p c d", c=HC),
                                                hot_w[0:HP, n % 2, :, 0:D], ALU.subtract).then_inc(hot_w_done, 1)

            def place_looked_up(k):
                for side in range(2):
                    if (k, side) not in DVE_PLACES:
                        continue
                    dve.wait_ge(hot_used, HC * (2 * k + side + 1))
                    for part, have in enumerate((slice(0, D), slice(D, P))):
                        for half in looked_up_halves(k, side):
                            last = nc.vector.tensor_copy(x[half, k % X_SLOTS, side, part, :],
                                                         u_ps[have, *looked_up_bank(2 * k + side), :])
                    last.then_inc(x_placed_dve, 1)

            def looked_up_whole(k):
                for side, own in enumerate((slice(0, D), slice(D, P))):
                    dve.wait_ge(*x_placed(k, side))
                    last = nc.vector.tensor_tensor(e_pair[own, k, :], x[own, k, side, 0, :],
                                                   x[own, k, side, 1, :], ALU.add)
                last.then_inc(looked_up_sum, 1)

            def split_low(k):
                if k - 2 >= HOT_BLOCKS:
                    for side in range(2):
                        dve.wait_ge(*x_placed(k - 2, side))
                dve.wait_ge(e_done, k + 1 - HOT_BLOCKS)
                nc.vector.tensor_tensor(e_split[:, k % 2, 1, :], e_pair[:, k, :], e_split[:, k % 2, 0, :],
                                        ALU.subtract).then_inc(e_low_done, 1)

            def place_weights(g):
                slot = g % W_SLOTS
                dve.wait_ge(raw_in[g // 2 % RAW_SLOTS], 16 * (g // 2 // RAW_SLOTS + 1))
                if g >= W_SLOTS:
                    dve.wait_ge(u_done, TG * (g - W_SLOTS + 1))
                for w, own in ((w_a, slice(0, D)), (w_b, slice(D, P))):
                    last = nc.vector.tensor_copy(w[own, slot, :], raw[own, g // 2 % RAW_SLOTS, g % 2, :])
                last.then_inc(high_placed_dve, 1)

            def place_fields(k):
                for side, own in enumerate((slice(0, D), slice(D, P))):
                    if (k, side) not in DVE_PLACES:
                        continue
                    if k >= X_SLOTS:
                        dve.wait_ge(u_done, LAST_USE[k - X_SLOTS] + 1)
                    dve.wait_ge(e_low_done, k + 1 - HOT_BLOCKS)
                    for half in (slice(0, D), slice(D, P)):
                        last = nc.vector.tensor_copy(x[half, k % X_SLOTS, side, :, :], e_split[own, k % 2, :, :])
                    last.then_inc(x_placed_dve, 1)

            for m, (k, j) in enumerate(TILES):
                for task, n in TASKS[m]:
                    if task == "weights":
                        if n not in POOL_LOWS:
                            weights_low(dve, nc.vector, n)
                        if n in DVE_HIGHS:
                            place_weights(n)
                    elif task == "place_fields":
                        place_fields(n)
                    elif task == "look_up":
                        look_up(n)
                    elif task == "place_looked_up":
                        place_looked_up(n)
                    elif task == "looked_up_whole":
                        looked_up_whole(n)
                    elif task == "split_low":
                        split_low(n)
                dve.wait_ge(u_done, m + 1)
                if m >= P_SLOTS:
                    dve.wait_ge(summed, FIRST_UNIT[m - P_SLOTS + 1])
                made, have = prod[:, m % P_SLOTS, :, :], u_ps[:, m % U_SLOTS, :, :]
                if j == "single":
                    dve.wait_ge(mixed_done, k // 2 + 1)
                    nc.vector.tensor_tensor(made[:, 1, :], have[:, 1, :], mixed[:, 1, :],
                                            ALU.mult).then_inc(prod_done, 1)
                elif j == "cross":
                    nc.vector.tensor_tensor(made[:, 0, :], have[:, 0, :], e_pair[:, k - 1, :], ALU.mult)
                    nc.vector.tensor_tensor(made[:, 1, :], have[:, 1, :], mixed[:, 0, :],
                                            ALU.mult).then_inc(prod_done, 1)
                else:
                    nc.vector.tensor_tensor(made, have, e_pair[:, j:j + 1, :].broadcast_to([P, 2, B]),
                                            ALU.mult).then_inc(prod_done, 1)

        @block.tensor
        def _(pe):
            def transpose_fields(k):
                if k == HOT_BLOCKS:
                    pe.wait_ge(consts_in, 4 * 16)
                pe.wait_ge(gathered[k], 2 * BT * 16)
                if k > HOT_BLOCKS:
                    pe.wait_ge(e_done, k - HOT_BLOCKS)
                for t in range(BT):
                    last = nc.tensor.transpose(t_ps[:, t * P:(t + 1) * P],
                                               rows[:, k % ROW_SLOTS, t, :, :].rearrange("p a d -> p (a d)"),
                                               ident_sb[:])
                last.then_inc(transposed, 1)

            def look_up(n):
                pe.wait_ge(hot_w_done, n + 1)
                for c in range(HC):
                    pe.wait_ge(hot_one_done, HC * n + c + 1)
                    nc.tensor.matmul(u_ps[:, *looked_up_bank(n), :], hot_w[0:HP, n % 2, c, :],
                                     hot_one[0:HP, c, :], start=c == 0, stop=c == HC - 1).then_inc(hot_used, 1)

            def multiply(m):
                g, slot = m // TG, m // TG % W_SLOTS
                pe.wait_ge(*high_placed(g))
                pe.wait_ge(low_placed[slot], 32 * (g // W_SLOTS + 1))
                if m < HOT_BLOCKS:
                    for side in range(2):
                        pe.wait_ge(*x_placed(m, side))
                if m >= U_SLOTS:
                    pe.wait_ge(prod_done, m - U_SLOTS + 1)
                cols = slice(m % TG * P, (m % TG + 1) * P)
                for side, c, _ in UNITS[m]:
                    if m == FIRST_USE[c]:
                        pe.wait_ge(*x_placed(c // 2, c % 2))
                    w = (w_a, w_b)[side]
                    for part in range(2):
                        last = nc.tensor.matmul(u_ps[:, m % U_SLOTS, side, :], w[:, slot, cols],
                                                x[:, c // 2 % X_SLOTS, side, part, :],
                                                start=part == 0, stop=part == 1)
                last.then_inc(u_done, 1)

            def sum_units(first, stop):
                for u in range(first, stop):
                    m, side = UNIT_AT[u]
                    bank, grp, row = z_place(u)
                    if u == 0:
                        pe.wait_ge(consts_in, 4 * 16)
                    if u == first or u == FIRST_UNIT[m]:
                        pe.wait_ge(prod_done, m + 1)
                    if u == BANK_UNITS * bank and bank > 0:
                        pe.wait_ge(bank_out, bank)
                    if u == BANK_UNITS * (BANKS - 1):
                        for q in range(GROUPS):
                            nc.tensor.matmul(z_ps[GROUP * q:GROUP * (q + 1), :], dense_sel_sb[:, q, :],
                                             dense_sb[:], start=True, stop=False)
                    last_row = u + GROUPS >= min(BANK_UNITS * (bank + 1), FIRST_UNIT[NT])
                    nc.tensor.matmul(z_ps[GROUP * grp:GROUP * (grp + 1), :],
                                     ones_sb[:, GROUP - 1 - row:2 * GROUP - 1 - row],
                                     prod[:, m % P_SLOTS, side, :],
                                     start=row == 0 and bank < BANKS - 1, stop=last_row).then_inc(summed, 1)

            def h1_part(q, n):
                return nc.tensor.matmul(h1_ps[:, n, :], w1_sb[:, q, n * P:(n + 1) * P], z[:, q, :],
                                        start=q == 0, stop=q == BANKS - 1)

            at = 0
            for m in range(NT):
                for task, n in TASKS[m]:
                    if task == "look_up":
                        look_up(n)
                    elif task == "transpose":
                        transpose_fields(n)
                multiply(m)
                if m > 1:
                    stop = FIRST_UNIT[m - 1 if m % 2 == 1 else m - 2]
                    if m % 2 == 1:
                        stop = min([BANK_UNITS * q for q in range(1, BANKS) if at < BANK_UNITS * q] + [stop])
                    sum_units(at, stop)
                    at = max(at, stop)
            pe.wait_ge(mlp_in, 5 * 16)
            pe.wait_ge(bank_out, BANKS - 1)
            pe.wait_ge(prod_done, NT - 1)
            early = [n for n in range(H1 // P) if n // 2 != (NT - 1) % U_SLOTS]
            for n in early:
                for q in range(BANKS - 1):
                    h1_part(q, n)
            sum_units(at, FIRST_UNIT[NT])
            for n in range(H1 // P):
                if n not in early:
                    for q in range(BANKS - 1):
                        h1_part(q, n)
            pe.wait_ge(bank_out, BANKS)
            for n in range(H1 // P):
                h1_part(BANKS - 1, n).then_inc(h1_acc, 1)
            for q in range(H1 // P):
                pe.wait_ge(h1_done, q + 1)
                for n in range(H2 // P):
                    last = nc.tensor.matmul(h2_ps[:, n, :], w2_sb[:, q, n * P:(n + 1) * P], h1[:, q, :],
                                            start=q == 0, stop=q == H1 // P - 1)
                    if q == H1 // P - 1:
                        last.then_inc(h2_acc, 1)
            for n in range(H2 // P):
                pe.wait_ge(h2_done, n + 1)
                last = nc.tensor.matmul(t_ps[0:1, :], w3_sb[:, n:n + 1], h2[:, n, :],
                                        start=n == 0, stop=n == H2 // P - 1)
            last.then_inc(y_acc, 1)
    return nc


def pair_index(r, c):
    return r * F - r * (r + 1) // 2 + c - r - 1


def field_order(table_rows):
    hot = [c for c in range(F) if table_rows[c] == HOT_ROWS][:HOT]
    return hot + [c for c in range(F) if c not in hot]


def z_rows(order):
    at = np.full(BANKS * P, -1)
    for m, units in enumerate(UNITS):
        for n, (_, c, rs) in enumerate(units):
            bank, grp, row = z_place(FIRST_UNIT[m] + n)
            for i, r in enumerate(rs):
                at[bank * P + GROUP * grp + row + i] = pair_index(*sorted((order[r], order[c])))
    at[at < 0] = F * (F - 1) // 2 + np.arange(DENSE)
    return at


def pack_weights(k3, order):
    packed = np.zeros((2, D, NT, 2, D), k3.dtype)
    for m, units in enumerate(UNITS):
        for side, c, rs in units:
            for n, r in enumerate(rs):
                row, col = order[r], order[c]
                pair = k3[:, pair_index(*sorted((row, col))), :]
                packed[side, :, m, n, :] = pair if row < col else pair.T
    return packed.reshape(P, NT * P)


def kernel(**inputs):
    import concourse.bacc as bacc
    from concourse.bass_utils import run_bass_kernel_spmd

    given = {n: np.ascontiguousarray(a) for n, a in inputs.items()}
    ones = np.zeros((P, 2 * GROUP), np.float32)
    ones[:D, GROUP - 1] = 1
    ones[D:, GROUP] = 1
    dense_sel = np.zeros((DENSE, GROUPS, GROUP), np.float32)
    per_group = DENSE // GROUPS
    for d in range(DENSE):
        dense_sel[d, d // per_group, GROUP - per_group + d % per_group] = 1
    order = field_order([given[f"tbl_{c}"].shape[0] for c in range(F)])
    arrays = {
        "ids": given["ids"],
        "hot_ids": np.ascontiguousarray(given["ids"][:, order[:HOT]].T),
        "hot_base": -float(HC) * np.arange(P, dtype=np.float32).reshape(P, 1),
    }
    for c in range(F):
        arrays[f"tbl_{c}"] = given[f"tbl_{c}"]
    arrays |= {
        "kp": pack_weights(given["L0_rec_kernel"], order),
        "w1": given["W_top1"][z_rows(order)],
        "b1": np.ascontiguousarray(given["b_top1"].reshape(H1 // P, P).T),
        "w2": given["W_top2"],
        "b2": np.ascontiguousarray(given["b_top2"].reshape(H2 // P, P).T),
        "w3": np.ascontiguousarray(given["W_top3"].reshape(H2 // P, P).T),
        "dense_t": np.ascontiguousarray(given["dense_ctx"].T),
        "ident": np.eye(P, dtype=np.float32),
        "ones": ones,
        "dense_sel": dense_sel,
    }
    nc = bacc.Bacc("TRN2", target_bir_lowering=False, num_devices=1)
    ap = {n: nc.dram_tensor(f"in_{n}", a.shape, mybir.dt.from_np(a.dtype), kind="ExternalInput").ap()
          for n, a in arrays.items()}
    out = nc.dram_tensor("out_y", (1, B), mybir.dt.float32, kind="ExternalOutput").ap()
    tables = [ap.pop(f"tbl_{c}") for c in range(F)]
    tower(nc, order, tables=tables, **ap, out=out)
    result = run_bass_kernel_spmd(nc, [{f"in_{n}": a for n, a in arrays.items()}], core_ids=[0])
    return np.asarray(result.results[0]["out_y"]).reshape(B, 1)
```
